# Optimizing a Trainium2 kernel written in Bass

```python
import numpy as np
import jax
import jax.numpy as jnp

def _softmax(x, axis=-1):
    return jax.nn.softmax(x, axis=axis)

def _gelu(x):
    return jax.nn.gelu(x, approximate=True)

def _silu(x):
    return jax.nn.silu(x)

def _sigmoid(x):
    return jax.nn.sigmoid(x)

def _layernorm(x, axis=-1, eps=1e-05):
    m = jnp.mean(x, axis=axis, keepdims=True)
    v = jnp.var(x, axis=axis, keepdims=True)
    return (x - m) / jnp.sqrt(v + eps)

def _scatter_add(tgt, idx, src, axis=0):
    return tgt.at[idx].add(src)

def _segment_sum(src, seg, n):
    return jax.ops.segment_sum(src, seg, n)
kernel_name = 'mk_adaln_ffn_d1_seqx_r4_6d815f'

def setup_inputs(seed: int=0):
    np.random.seed(seed)
    _w = jnp.asarray

    def _rec_inputs():
        import jax
        import jax.numpy as jnp
        _rk = jax.random.key(seed)
        x = -0.000125 + 0.9999 * jax.random.normal(jax.random.fold_in(_rk, 1), (64, 64, 256), jnp.float32)
        _lenS = 64 - jax.random.randint(jax.random.fold_in(_rk, 7), (64,), 0, max(1, 64 // 4) + 1, jnp.int32)
        _lenS2 = 64 - jax.random.randint(jax.random.fold_in(_rk, 8), (64,), 0, max(1, 64 // 4) + 1, jnp.int32)
        cond_512 = 0.0061147 + 1.02565 * jax.random.normal(jax.random.fold_in(_rk, 11), (64, 128), jnp.float32)
        return (x, cond_512)
    x, cond_512 = _rec_inputs()

    def _L0_cond_setup():
        import jax, jax.numpy as jnp
        import numpy as np
        B, S, D, H, C = (8, 1024, 256, 64, 128)
        INIT_RANGE = 0.01
        key = jax.random.key(seed)
        ks = jax.random.split(key, 6)
        return {'hidden_states': jax.random.normal(ks[0], (B, S, D), dtype=jnp.float32), 'conditions': jax.random.normal(ks[1], (B, C), dtype=jnp.float32), 'down_project': jax.random.normal(ks[2], (D, H), dtype=jnp.float32) * INIT_RANGE, 'down_gamma': jax.random.normal(ks[3], (C, H), dtype=jnp.float32), 'down_beta': jnp.zeros((C, H), dtype=jnp.float32), 'up_project': jax.random.normal(ks[4], (H, D), dtype=jnp.float32) * INIT_RANGE, 'up_gamma': jax.random.normal(ks[5], (C, D), dtype=jnp.float32), 'up_beta': jnp.zeros((C, D), dtype=jnp.float32)}
    _L0_cond_all = _L0_cond_setup()
    _L0_cond_in = {k: v for k, v in _L0_cond_all.items() if k in ('down_project', 'down_gamma', 'down_beta', 'up_project', 'up_gamma', 'up_beta')}
    del _L0_cond_all

    def _L0_ffn_setup():
        import math
        import jax
        import jax.numpy as jnp
        import numpy as np
        B, T, D = (1, 512, 256)
        H, KV, DH = (16, 4, 64)
        E, TOPK, DFF = (32, 4, 256)
        WINDOW = 128
        EPS = 1e-05
        ROPE_BASE = 150000.0
        ROPE_SCALE = 32.0

        def _rmsnorm(x, w):
            rms = jax.lax.rsqrt(jnp.mean(x * x, axis=-1, keepdims=True) + EPS)
            return w * (x * rms)

        def _apply_rope(x, sin, cos):
            x1, x2 = (x[..., ::2], x[..., 1::2])
            out = jnp.stack([x1 * cos - x2 * sin, x1 * sin + x2 * cos], axis=-1)
            return out.reshape(x.shape)
        key = jax.random.key(seed)
        ks = jax.random.split(key, 12)
        s = 0.02
        return {'x': jax.random.normal(ks[0], (B, T, D), jnp.float32), 'attn_norm_w': 1.0 + 0.02 * jax.random.normal(ks[1], (D,), jnp.float32), 'ffn_norm_w': 1.0 + 0.02 * jax.random.normal(ks[2], (D,), jnp.float32), 'qkv_w': s * jax.random.normal(ks[3], (D, H * DH + 2 * KV * DH), jnp.float32), 'qkv_b': s * jax.random.normal(ks[4], (H * DH + 2 * KV * DH,), jnp.float32), 'proj_w': s * jax.random.normal(ks[5], (H * DH, D), jnp.float32), 'proj_b': s * jax.random.normal(ks[6], (D,), jnp.float32), 'attn_sink': 0.5 * jax.random.normal(ks[7], (H,), jnp.float32), 'gate_w': s * jax.random.normal(ks[8], (D, E), jnp.float32), 'gate_b': s * jax.random.normal(ks[9], (E,), jnp.float32), 'W_up': s * jax.random.normal(ks[10], (E, D, 2 * DFF), jnp.float32), 'W_down': s * jax.random.normal(ks[11], (E, DFF, D), jnp.float32)}
    _L0_ffn_all = _L0_ffn_setup()
    _L0_ffn_in = {k: v for k, v in _L0_ffn_all.items() if k in ('attn_norm_w', 'ffn_norm_w', 'qkv_w', 'qkv_b', 'proj_w', 'proj_b', 'attn_sink', 'gate_w', 'gate_b', 'W_up', 'W_down')}
    del _L0_ffn_all
    return {'x': x, 'cond_512': cond_512, 'L0_cond_down_project': _L0_cond_in['down_project'], 'L0_cond_down_gamma': _L0_cond_in['down_gamma'], 'L0_cond_down_beta': _L0_cond_in['down_beta'], 'L0_cond_up_project': _L0_cond_in['up_project'], 'L0_cond_up_gamma': _L0_cond_in['up_gamma'], 'L0_cond_up_beta': _L0_cond_in['up_beta'], 'L0_ffn_attn_norm_w': _L0_ffn_in['attn_norm_w'], 'L0_ffn_ffn_norm_w': _L0_ffn_in['ffn_norm_w'], 'L0_ffn_qkv_w': _L0_ffn_in['qkv_w'], 'L0_ffn_qkv_b': _L0_ffn_in['qkv_b'], 'L0_ffn_proj_w': _L0_ffn_in['proj_w'], 'L0_ffn_proj_b': _L0_ffn_in['proj_b'], 'L0_ffn_attn_sink': _L0_ffn_in['attn_sink'], 'L0_ffn_gate_w': _L0_ffn_in['gate_w'], 'L0_ffn_gate_b': _L0_ffn_in['gate_b'], 'L0_ffn_W_up': _L0_ffn_in['W_up'], 'L0_ffn_W_down': _L0_ffn_in['W_down']}

def reference(x, cond_512, L0_cond_down_project, L0_cond_down_gamma, L0_cond_down_beta, L0_cond_up_project, L0_cond_up_gamma, L0_cond_up_beta, L0_ffn_attn_norm_w, L0_ffn_ffn_norm_w, L0_ffn_qkv_w, L0_ffn_qkv_b, L0_ffn_proj_w, L0_ffn_proj_b, L0_ffn_attn_sink, L0_ffn_gate_w, L0_ffn_gate_b, L0_ffn_W_up, L0_ffn_W_down):
    import jax
    import jax.numpy as jnp

    def _L0_cond_ref(hidden_states, conditions, down_project, down_gamma, down_beta, up_project, up_gamma, up_beta):
        import jax, jax.numpy as jnp
        import numpy as np
        B, S, D, H, C = (8, 1024, 256, 64, 128)
        INIT_RANGE = 0.01
        dg = conditions @ down_gamma
        db = conditions @ down_beta
        ug = conditions @ up_gamma
        ub = conditions @ up_beta
        w_down = down_project[None, :, :] * dg[:, None, :] + db[:, None, :]
        down = jnp.einsum('bsd,bdh->bsh', hidden_states, w_down)
        act = jax.nn.relu(down)
        w_up = up_project[None, :, :] * ug[:, None, :] + ub[:, None, :]
        up = jnp.einsum('bsh,bhd->bsd', act, w_up)
        return up + hidden_states

    def _L0_ffn_ref(x, attn_norm_w, ffn_norm_w, qkv_w, qkv_b, proj_w, proj_b, attn_sink, gate_w, gate_b, W_up, W_down):
        import math
        import jax
        import jax.numpy as jnp
        import numpy as np
        B, T, D = (1, 512, 256)
        H, KV, DH = (16, 4, 64)
        E, TOPK, DFF = (32, 4, 256)
        WINDOW = 128
        EPS = 1e-05
        ROPE_BASE = 150000.0
        ROPE_SCALE = 32.0

        def _rmsnorm(x, w):
            rms = jax.lax.rsqrt(jnp.mean(x * x, axis=-1, keepdims=True) + EPS)
            return w * (x * rms)

        def _apply_rope(x, sin, cos):
            x1, x2 = (x[..., ::2], x[..., 1::2])
            out = jnp.stack([x1 * cos - x2 * sin, x1 * sin + x2 * cos], axis=-1)
            return out.reshape(x.shape)
        Bx, Tx, Dx = x.shape
        h = _rmsnorm(x, attn_norm_w)
        qkv = h @ qkv_w + qkv_b
        q = qkv[..., :H * DH].reshape(Bx, Tx, H, DH).transpose(0, 2, 1, 3)
        k = qkv[..., H * DH:H * DH + KV * DH].reshape(Bx, Tx, KV, DH).transpose(0, 2, 1, 3)
        v = qkv[..., H * DH + KV * DH:].reshape(Bx, Tx, KV, DH).transpose(0, 2, 1, 3)
        pos = jnp.arange(Tx, dtype=jnp.float32) / ROPE_SCALE
        inv_freq = 1.0 / ROPE_BASE ** (jnp.arange(0, DH, 2, dtype=jnp.float32) / DH)
        freqs = pos[:, None] * inv_freq[None, :]
        sin, cos = (jnp.sin(freqs), jnp.cos(freqs))
        q = _apply_rope(q, sin, cos)
        k = _apply_rope(k, sin, cos)
        rep = H // KV
        k = jnp.repeat(k, rep, axis=1)
        v = jnp.repeat(v, rep, axis=1)
        logits = jnp.einsum('bhqd,bhkd->bhqk', q, k) / math.sqrt(DH)
        i = jnp.arange(Tx)[:, None]
        j = jnp.arange(Tx)[None, :]
        mask = (j > i) | (i - j > WINDOW)
        logits = jnp.where(mask, -jnp.inf, logits)
        lse = jax.nn.logsumexp(logits, axis=-1, keepdims=True)
        denom_log = jnp.logaddexp(lse, attn_sink.reshape(1, H, 1, 1))
        attn = jnp.exp(logits - denom_log)
        y = jnp.einsum('bhqk,bhkd->bhqd', attn, v)
        y = y.transpose(0, 2, 1, 3).reshape(Bx, Tx, H * DH)
        x = x + (y @ proj_w + proj_b)
        h2 = _rmsnorm(x, ffn_norm_w).reshape(Bx * Tx, Dx)
        glogits = h2 @ gate_w + gate_b
        topv, topi = jax.lax.top_k(glogits, TOPK)
        gw = jax.nn.softmax(topv, axis=-1)
        N = Bx * Tx
        combine = jnp.zeros((N, E), x.dtype).at[jnp.arange(N)[:, None], topi].add(gw)

        def body(acc, we):
            wu, wd, ce = we
            ug = h2 @ wu
            u, g = (ug[:, :DFF], ug[:, DFF:])
            return (acc + ce[:, None] * (jax.nn.silu(g) * u @ wd), None)
        y2, _ = jax.lax.scan(body, jnp.zeros_like(h2), (W_up, W_down, combine.T))
        return x + y2.reshape(Bx, Tx, Dx)
    x = x + _L0_ffn_ref(_L0_cond_ref(x, cond_512, L0_cond_down_project, L0_cond_down_gamma, L0_cond_down_beta, L0_cond_up_project, L0_cond_up_gamma, L0_cond_up_beta), L0_ffn_attn_norm_w, L0_ffn_ffn_norm_w, L0_ffn_qkv_w, L0_ffn_qkv_b, L0_ffn_proj_w, L0_ffn_proj_b, L0_ffn_attn_sink, L0_ffn_gate_w, L0_ffn_gate_b, L0_ffn_W_up, L0_ffn_W_down)
    return x

_drawn_inputs = setup_inputs


def setup_inputs(seed=0):
    import zlib

    import numpy as np

    out = dict(_drawn_inputs(seed))
    spreads = {'L0_cond_down_beta': (0.0, 0.1), 'L0_cond_up_beta': (0.0, 0.1)}
    factors = {'L0_cond_down_project': 2.7,
     'L0_cond_down_gamma': 2.726,
     'L0_cond_up_gamma': 2.7,
     'L0_ffn_attn_norm_w': 8.0,
     'L0_ffn_ffn_norm_w': 8.0,
     'L0_ffn_qkv_w': 8.0,
     'L0_ffn_qkv_b': 8.0,
     'L0_ffn_proj_w': 8.0,
     'L0_ffn_proj_b': 200.0,
     'L0_ffn_attn_sink': 8.0,
     'L0_ffn_gate_w': 8.0,
     'L0_ffn_gate_b': 8.0,
     'L0_ffn_W_up': 8.0,
     'L0_ffn_W_down': 8.0}
    for name, (base, spread) in spreads.items():
        noise = np.random.default_rng([zlib.crc32(name.encode()), seed]).standard_normal(out[name].shape)
        drawn = base * np.exp(spread * noise) if base else spread * noise
        out[name] = jnp.asarray(drawn.astype(out[name].dtype))
    for name, factor in factors.items():
        out[name] = (out[name] * factor).astype(out[name].dtype)
    return out
```

```python
from contextlib import ExitStack

import numpy as np

import concourse.bass as bass
from concourse import mybir
from concourse.alu_op_type import AluOpType as ALU

F32, I32, U32, BF16 = mybir.dt.float32, mybir.dt.int32, mybir.dt.uint32, mybir.dt.bfloat16
ACT = mybir.ActivationFunctionType
AX = mybir.AxisListType

P = 128
NSEQ, T, D = 64, 64, 256
NTOK = NSEQ * T
CH = 64
H, KV, DH = 16, 4, 64
REP = H // KV
E, TOPK, DFF = 32, 4, 256
EPS = 1e-5
KC = D // P
FC = DFF // P
MT = 512
NM = NTOK // MT
MS = MT // T
TPM = MT // P
NT = NTOK // P
NPAIR = REP + 1
LIST = NTOK
LT = LIST // P
PAIRS = NTOK * TOPK
NET = PAIRS // P + E - 1
NET2 = 32 * -(-(NET - P) // 32)
RING = 4
WE = KC * 2 * DFF + FC * D
NEG = -1e30


class Plan:

    def __init__(self):
        self.lanes = {}
        self.done = {}

    def put(self, lane, name, after, emit, sem=None, inc=1, total=None):
        self.lanes.setdefault(lane, []).append((name, list(after), emit, sem, inc))
        if sem is not None and name is not None:
            self.done[name] = (sem, total)

    def settle(self, engine_sem):
        wanted = {n for items in self.lanes.values() for _, after, *_ in items for n in after}
        for lane, items in self.lanes.items():
            count = 0
            for name, _, _, sem, _ in items:
                if sem is None and name in wanted:
                    count += 1
                    assert name not in self.done, name
                    self.done[name] = (engine_sem[lane], count)
        self.wanted, self.engine_sem = wanted, engine_sem

    def emit(self, lane, eng):
        passed = {}
        for name, after, emit, sem, inc in self.lanes[lane]:
            need = {}
            for n in after:
                s, v = self.done[n]
                need[s.name] = max(need.get(s.name, (0, s))[0], v), s
            for key, (v, s) in need.items():
                if passed.get(key, 0) < v:
                    eng.wait_ge(s, v)
                    passed[key] = v
            ins = emit(eng)
            if sem is not None:
                ins.then_inc(sem, inc)
            elif name in self.wanted:
                ins.then_inc(self.engine_sem[lane], 1)


class Banks:

    def __init__(self, banks):
        self.banks, self.n, self.readers = banks, 0, {}

    def take(self):
        u = self.n
        self.n += 1
        return u, self.banks[u % len(self.banks)], self.readers.get(u - len(self.banks), [])

    def read_by(self, u, *names):
        self.readers[u] = list(names)


def program(nc, d):
    ctx = ExitStack()
    part1 = ExitStack()

    def sb(name, shape, dt=F32, stack=ctx):
        return stack.enter_context(nc.sbuf_tensor(name, shape, dt))

    def sem(name):
        return ctx.enter_context(nc.semaphore(name))

    h2_rows = nc.dram_tensor("h2_rows", (NTOK, D), F32, kind="Internal").ap()
    lists = nc.dram_tensor("lists", (E * LIST + P, 2), F32, kind="Internal").ap()
    pick_rows = nc.dram_tensor("pick_rows", (PAIRS, D), F32, kind="Internal").ap()

    plan = Plan()

    def pe(name, after, emit):
        plan.put("tensor", name, after, emit)

    def dve(name, after, emit):
        plan.put("vector", name, after, emit)

    def act(name, after, emit):
        plan.put("scalar", name, after, emit)

    def pool(name, after, emit):
        plan.put("gpsimd", name, after, emit)

    def dma(lane, name, after, sem_, total, out, in_):
        plan.put(lane, name, after, lambda e: e.dma_start(out, in_), sem_, 16, total)

    resid = sb("resid", [P, NT, D])
    ring = sb("ring", [P, RING * WE])
    ident = sb("ident", [P, P])
    tile_no = sb("tile_no", [P, 2])
    list_base = sb("list_base", [P, E])
    fill_slots = sb("fill_slots", [P, P, 2])
    filled = sb("filled", [P, E])

    def sb1(name, shape, dt=F32):
        return sb(name, shape, dt, part1)

    w_qk = sb1("w_qk", [P, KC, NPAIR * 2, P])
    w_v = sb1("w_v", [P, KC, KV * DH])
    w_o = sb1("w_o", [P, H * DH // P, D])
    w_gate = sb1("w_gate", [P, KC, E])
    norm1_w = sb1("norm1_w", [P, KC])
    norm2_w = sb1("norm2_w", [P, D])
    b_qk = sb1("b_qk", [P, NPAIR * 2])
    b_v = sb1("b_v", [P, KV * DH])
    b_o = sb1("b_o", [P, D])
    b_gate = sb1("b_gate", [P, E])
    sink = sb1("sink", [P, 4, 4])
    w_down_ones = sb1("w_down_ones", [P, KC, P])
    w_up_ones = sb1("w_up_ones", [CH, D + P])
    cond_t = sb1("cond_t", [P, NSEQ])
    g_down = sb1("g_down", [P, P])
    g_up = sb1("g_up", [P, 2 * D])
    c_down = sb1("c_down", [P, NSEQ])
    c_up = sb1("c_up", [P, 4, NSEQ])
    rope = sb1("rope", [P, 4, T])
    causal = sb1("causal", [P, 4, T], BF16)
    causal_f = sb1("causal_f", [P, T])
    ident_b = sb1("ident_b", [P, P], BF16)
    earlier_f = sb1("earlier_f", [P, P])
    earlier = sb1("earlier", [P, P], BF16)
    ones_b = sb1("ones_b", [P, P], BF16)
    ones = sb1("ones", [P, P])
    eps = sb1("eps", [P, 1])
    expert_no = sb1("expert_no", [P, E])
    pair_no = sb1("pair_no", [P, TOPK])

    x_t = [sb1(f"x_t{i}", [P, KC, MT]) for i in range(2)]
    x0_t = [sb1(f"x0_t{i}", [P, KC, MT]) for i in range(2)]
    h_t = sb1("h_t", [P, KC, MT])
    tmp = [[sb1(f"tmp{i}{j}", [P, MT]) for j in range(4)] for i in range(2)]
    q_r = [sb1(f"q_r{i}", [P, 2, MS, REP, T]) for i in range(2)]
    k_r = [sb1(f"k_r{i}", [P, 2, MT]) for i in range(2)]
    v_s = [sb1(f"v_s{i}", [P, TPM, KV * DH]) for i in range(2)]
    prob = [sb1(f"prob{i}", [P, 16, T]) for i in range(2)]
    prob_t = sb1("prob_t", [P, KV, REP * T])
    y_t = sb1("y_t", [P, 2, REP, 2, T])
    stat = [sb1(f"stat{i}", [P, 5, 16]) for i in range(2)]
    x2 = [sb1(f"x2_{i}", [P, TPM, D]) for i in range(2)]
    ssq = [sb1(f"ssq{i}", [P, TPM]) for i in range(2)]
    rms2 = [sb1(f"rms2_{i}", [P, TPM]) for i in range(2)]
    h2 = [sb1(f"h2_{i}", [P, D]) for i in range(2)]
    h2_t = sb1("h2_t", [P, KC, P])
    sq_scrap = sb1("sq_scrap", [P, D])
    glog = sb1("glog", [P, E])
    top = sb1("top", [P, 8])
    top_i = sb1("top_i", [P, 8], U32)
    top_f = sb1("top_f", [P, TOPK])
    gexp = sb1("gexp", [P, TOPK])
    gsum = sb1("gsum", [P, 2])
    onehot = sb1("onehot", [P, TOPK, E])
    onehot_s = sb1("onehot_s", [P, TOPK, E])
    picked = sb1("picked", [P, E], BF16)
    rank = sb1("rank", [P, E])
    slot_f = sb1("slot_f", [P, TOPK])
    NPAY = 4
    slot_i = [sb1(f"slot_i{i}", [P, TOPK], I32) for i in range(NPAY)]
    entry = [sb1(f"entry{i}", [P, TOPK, 2]) for i in range(NPAY)]

    gbank = [ctx.enter_context(nc.psum_tensor(f"gbank{i}", [P, 512], F32)) for i in range(4)]
    scores = ctx.enter_context(nc.psum_tensor("scores", [P, 4, 512], F32))
    banks = Banks(gbank)

    engine_sem = {k: sem(f"s_{k}") for k in ("tensor", "vector", "scalar", "gpsimd", "sync")}
    s_const, s_const2 = sem("s_const"), sem("s_const2")
    s_xt = [sem(f"s_xt{i}") for i in range(2)]
    s_res = sem("s_res")
    s_fill = sem("s_fill")
    s_h2 = [sem(f"s_h2_{i}") for i in range(2)]
    s_entry = [sem(f"s_entry{i}") for i in range(NPAY)]

    early = [
        (cond_t[:, :], d["cond_t"]), (g_down[:, 0:CH], d["g_down"]), (g_down[:, CH:P], d["b_down"]),
        (g_up[:, 0:D], d["g_up"]), (g_up[:, D:2 * D], d["b_up"]),
        (w_down_ones[:, :, 0:CH], d["w_down"].rearrange("(c p) n -> p c n", p=P)),
        (w_up_ones[:, 0:D], d["w_up"]), (norm1_w[:, :], d["norm1_w"]),
        (w_qk[:, :, :, :], d["w_qk"].rearrange("(c p) (b n) -> p c b n", p=P, n=P)),
        (b_qk[:, :], d["b_qk"]), (rope[:, :, :], d["rope"]),
        (w_v[:, :, :], d["w_v"].rearrange("(c p) n -> p c n", p=P)), (b_v[:, :], d["b_v"]),
    ]
    late = [
        (causal_f[:, :], d["causal"]), (ident[:, :], d["ident"]), (sink[:, :, :], d["sink"]),
        (w_o[:, :, :], d["w_o"].rearrange("(c p) n -> p c n", p=P)), (b_o[:, :], d["b_o"]),
        (norm2_w[:, :], d["norm2_w"]), (w_gate[:, :, :], d["w_gate"].rearrange("(c p) n -> p c n", p=P)),
        (b_gate[:, :], d["b_gate"]), (earlier_f[:, :], d["earlier"]), (expert_no[:, :], d["expert_no"]),
        (list_base[:, :], d["list_base"]), (filled[:, :], d["list_base"]), (pair_no[:, :], d["pair_no"]),
        (tile_no[:, :], d["tile_no"]), (fill_slots[:, :, :], d["fill_slots"]),
    ]

    def load_x_t(m):
        dma("sync", ("x_t", m), [("x0", m - 2, KC - 1), ("down", m - 2)] if m >= 2 else [],
            s_xt[m % 2], 16 * (m // 2 + 1), x_t[m % 2][:, :, :],
            d["x_t"][:, m * MT:(m + 1) * MT].rearrange("(c p) n -> p c n", p=P))

    load_x_t(0)
    for n, (dst, src) in enumerate(early):
        dma("sync" if n % 2 else "scalar", "early", [], s_const, 16 * len(early), dst, src)
    load_x_t(1)
    for n, (dst, src) in enumerate(late):
        dma("sync", "late", [], s_const2, 16 * len(late), dst, src)
    dma("sync", "resid_x", [], s_res, 16, resid[:, :, :], d["x"].rearrange("(t p) n -> p t n", p=P))
    for c in range(E * LT // P):
        dma("sync", "fill", ["late"], s_fill, 16 * (E * LT // P + 1),
            lists[c * P * P:(c + 1) * P * P, :].rearrange("(t r) w -> t (r w)", r=P),
            fill_slots[:, :, :].rearrange("p r w -> p (r w)"))
    dma("sync", "fill", ["late"], s_fill, 16 * (E * LT // P + 1),
        lists[E * LIST:E * LIST + P, :].rearrange("(t r) w -> t (r w)", r=P),
        fill_slots[0:1, :, :].rearrange("p r w -> p (r w)"))

    pool(None, [], lambda e: e.memset(w_down_ones[:, :, CH:P], 1.0))
    pool(None, [], lambda e: e.memset(w_up_ones[:, D:D + P], 1.0))
    pool(None, [], lambda e: e.memset(ones[:, :], 1.0))
    pool(None, [], lambda e: e.memset(ones_b[:, :], 1.0))
    pool("ones", [], lambda e: e.memset(eps[:, :], EPS))
    for c in range(KC):
        dve(("w_qk", c), ["early"], lambda e, c=c: e.tensor_scalar(
            w_qk[:, c, :, :], w_qk[:, c, :, :], norm1_w[:, c:c + 1], None, ALU.mult))
        dve(("w_v", c), ["early"], lambda e, c=c: e.tensor_scalar(
            w_v[:, c, :], w_v[:, c, :], norm1_w[:, c:c + 1], None, ALU.mult))
    for r in range(4):
        dve("causal", ["late"], lambda e, r=r: e.tensor_copy(causal[:, r, :], causal_f[:, :])) \
            if r == 3 else dve(None, ["late"], lambda e, r=r: e.tensor_copy(causal[:, r, :], causal_f[:, :]))
    dve(None, ["late"], lambda e: e.tensor_copy(ident_b[:, :], ident[:, :]))
    dve("consts_b", ["late"], lambda e: e.tensor_copy(earlier[:, :], earlier_f[:, :]))

    u, bank, free = banks.take()
    pe(None, ["early"] + free, lambda e, b=bank: e.matmul(
        b[:, 0:NSEQ], g_down[:, :], cond_t[:, :], start=True, stop=True))
    for c in range(4):
        pe("c_all" if c == 3 else None, [], lambda e, b=bank, c=c: e.matmul(
            b[:, (c + 1) * NSEQ:(c + 2) * NSEQ], g_up[:, c * P:(c + 1) * P], cond_t[:, :], start=True, stop=True))
    dve("c_down", ["c_all"], lambda e, b=bank: e.tensor_copy(c_down[:, :], b[:, 0:NSEQ]))
    dve("c_up", ["c_all"], lambda e, b=bank: e.tensor_copy(
        c_up[:, :, :], b[:, NSEQ:5 * NSEQ].rearrange("p (c n) -> p c n", c=4)))
    banks.read_by(u, "c_up", "c_down")

    def by_seq(ap):
        return ap.rearrange("p (b s) -> p b s", s=T)

    def down(m):
        i = m % 2
        d_mul, d_add, d_sum, d_act = tmp[0]
        u, bank, free = banks.take()
        for c in range(KC):
            pe(("down", m) if c == KC - 1 else None, [("x_t", m), "early", "ones"] + free,
               lambda e, b=bank, c=c: e.matmul(b[:, :], w_down_ones[:, c, :], x_t[i][:, c, :],
                                               start=c == 0, stop=c == KC - 1))
        before = [("down", m), "c_down"] + ([("q_add", m - 1, 4)] if m else [])
        seqs = slice(m * MS, (m + 1) * MS)
        dve(None, before, lambda e, b=bank: e.tensor_tensor(
            by_seq(d_mul[0:CH, :]), by_seq(b[0:CH, :]),
            c_down[0:CH, seqs].unsqueeze(2).to_broadcast([CH, MS, T]), ALU.mult))
        dve(("d_mul", m), [], lambda e, b=bank: e.tensor_tensor(
            by_seq(d_add[0:CH, :]), by_seq(b[CH:P, :]),
            c_down[CH:P, seqs].unsqueeze(2).to_broadcast([CH, MS, T]), ALU.mult))
        banks.read_by(u, ("d_mul", m))
        dve(("d_sum", m), [("d_mul", m)], lambda e: e.tensor_tensor(
            d_sum[0:CH, :], d_mul[0:CH, :], d_add[0:CH, :], ALU.add))
        act(("act", m), [("d_sum", m)], lambda e: e.activation(d_act[0:CH, :], d_sum[0:CH, :], ACT.Relu))

    def up(m):
        i = m % 2
        d_act = tmp[0][3]
        seqs = slice(m * MS, (m + 1) * MS)
        took = []
        for c in range(KC + 1):
            u, bank, free = banks.take()
            took.append((u, bank))
            pe(("up", m, c), [("act", m)] + free, lambda e, b=bank, c=c: e.matmul(
                b[:, :], w_up_ones[:, c * P:(c + 1) * P], d_act[0:CH, :], start=True, stop=True))
        sums = took[KC][1]
        for c in range(KC):
            t_mul, t_add = tmp[1][2 * c], tmp[1][2 * c + 1]
            dve(("u_mul", m, c), [("up", m, c), "c_up"] + ([("q_add", m - 1, 4)] if m else []),
                lambda e, b=took[c][1], c=c, t=t_mul: e.tensor_tensor(
                    by_seq(t[:, :]), by_seq(b[:, :]),
                    c_up[:, c, seqs].unsqueeze(2).to_broadcast([P, MS, T]), ALU.mult))
            banks.read_by(took[c][0], ("u_mul", m, c))
            dve(("u_add", m, c), [("up", m, KC)], lambda e, c=c, t=t_add: e.tensor_tensor(
                by_seq(t[:, :]), by_seq(sums[:, :]),
                c_up[:, KC + c, seqs].unsqueeze(2).to_broadcast([P, MS, T]), ALU.mult))
            pool(("u_sum", m, c), [("u_mul", m, c), ("u_add", m, c)], lambda e, a=t_mul, b=t_add: e.tensor_tensor(
                a[:, :], a[:, :], b[:, :], ALU.add))
        banks.read_by(took[KC][0], ("u_add", m, KC - 1))
        for c in range(KC):
            dve(("x0", m, c), [("u_sum", m, c)] + ([("proj", TPM * (m - 1) - 1)] if m >= 2 else []),
                lambda e, c=c, a=tmp[1][2 * c]: e.tensor_tensor(
                    x0_t[i][:, c, :], a[:, :], x_t[i][:, c, :], ALU.add))
            act(("sq", m, c), [("x0", m, c), ("up", m, KC)], lambda e, c=c: e.activation(
                tmp[0][c][:, :], x0_t[i][:, c, :], ACT.Square))

    def norm1(m):
        i = m % 2
        root, rms = tmp[0][2], tmp[0][3]
        u, bank, free = banks.take()
        for c in range(KC):
            pe(("ssq1", m) if c == KC - 1 else None, [("sq", m, c)] + free, lambda e, b=bank, c=c: e.matmul(
                b[:, :], ones[:, :], tmp[0][c][:, :], start=c == 0, stop=c == KC - 1))
        act(("root1", m), [("ssq1", m), ("d_sum", m), "ones"], lambda e, b=bank: e.activation(
            root[:, :], b[:, :], ACT.Sqrt, bias=eps[:, 0:1], scale=1.0 / D))
        banks.read_by(u, ("root1", m))
        if m >= 2:
            root2(m - 2)
        dve(("rms1", m), [("root1", m)], lambda e: e.reciprocal(rms[:, :], root[:, :]))
        for c in range(KC):
            dve(("h", m, c), [("rms1", m)] + ([("v", m - 1, TPM - 1)] if m else []), lambda e, c=c: e.tensor_tensor(
                h_t[:, c, :], x0_t[i][:, c, :], rms[:, :], ALU.mult))

    def pair(m, j):
        i = m % 2
        t = tmp[j % 2]
        took = []
        for o in range(2):
            u, bank, free = banks.take()
            took.append((u, bank))
            for c in range(KC):
                pe(("qk", m, j, o) if c == KC - 1 else None, [("h", m, c), ("w_qk", c)] + free,
                   lambda e, b=bank, c=c, o=o: e.matmul(
                       b[:, :], w_qk[:, c, 2 * j + o, :], h_t[:, c, :], start=c == 0, stop=c == KC - 1))
        trig = 0 if j < REP else 2
        last = ("q_add", m, j - 2) if j >= 2 else ("h", m, KC - 1)
        for n, (o, s) in enumerate(((0, 0), (1, 1), (0, 1), (1, 0))):
            dve(("q_mul", m, j, n), [("qk", m, j, o), last], lambda e, n=n, o=o, s=s: e.scalar_tensor_tensor(
                out=by_seq(t[n][:, :]), in0=by_seq(took[o][1][:, :]), scalar=b_qk[:, 2 * j + o:2 * j + o + 1],
                in1=rope[:, trig + s:trig + s + 1, :].to_broadcast([P, MS, T]), op0=ALU.add, op1=ALU.mult))
        banks.read_by(took[0][0], ("q_mul", m, j, 2))
        banks.read_by(took[1][0], ("q_mul", m, j, 3))
        if j < REP:
            dst = [q_r[i][:, o, :, j, :] for o in range(2)]
        else:
            dst = [by_seq(k_r[i][:, o, :]) for o in range(2)]
        free = [("scores", TPM * (m - 1) - 1)] if m >= 2 else []
        pool(None, [("q_mul", m, j, 1)] + free, lambda e: e.tensor_tensor(
            dst[0], by_seq(t[0][:, :]), by_seq(t[1][:, :]), ALU.subtract))
        pool(("q_add", m, j), [("q_mul", m, j, 3)], lambda e: e.tensor_tensor(
            dst[1], by_seq(t[2][:, :]), by_seq(t[3][:, :]), ALU.add))

    def value(m, s):
        i = m % 2
        u, bank, free = banks.take()
        for c in range(KC):
            pe(("v", m, s) if c == KC - 1 else None, [("h", m, c), ("w_v", c)] + free, lambda e, b=bank, c=c: e.matmul(
                b[:, 0:KV * DH], h_t[:, c, s * P:(s + 1) * P], w_v[:, c, :], start=c == 0, stop=c == KC - 1))
        dve(("v_s", m, s), [("v", m, s)] + ([("pv", TPM * (m - 2) + s)] if m >= 2 else []),
            lambda e, b=bank: e.tensor_tensor(v_s[i][:, s, :], b[:, 0:KV * DH], b_v[:, :], ALU.add))
        banks.read_by(u, ("v_s", m, s))

    def score_view(t):
        return scores[:, :, 0:4 * T].rearrange("p g (a k) -> p g a k", k=T)

    def score(t):
        m, s = divmod(t, TPM)
        i = m % 2
        free = [("shift", t - 1)] if t else []
        for g in range(KV):
            pe(None, ["causal", "consts_b"] + free, lambda e, g=g: e.matmul(
                scores[:, g, 0:4 * T], ident_b[:, :], causal[:, :, :].rearrange("p a k -> p (a k)"),
                start=True, stop=False, skip_group_check=True))
        for n, (a, b, o) in enumerate((a, b, o) for a in range(2) for b in range(2) for o in range(2)):
            for g in range(KV):
                rows = slice(32 * g, 32 * g + 32)
                col = (2 * a + b) * T
                pe(("scores", t) if n == 7 and g == KV - 1 else None, [("q_add", m, j) for j in range(NPAIR)],
                   lambda e, g=g, a=a, b=b, o=o, rows=rows, col=col: e.matmul(
                       scores[:, g, col:col + T],
                       q_r[i][rows, o, 2 * s + b, 2 * a:2 * a + 2, :].rearrange("p j s -> p (j s)"),
                       k_r[i][rows, o, (2 * s + b) * T:(2 * s + b + 1) * T],
                       start=False, stop=o == 1, skip_group_check=True, tile_position=(32 * g, 0)))

    def softmax_a(t):
        st, pr = stat[t % 2], prob[t % 2]
        four = lambda ap: ap.rearrange("p (g a) -> p g a", g=4)
        dve(("rowmax", t), [("scores", t)], lambda e: e.tensor_reduce(
            four(st[:, 0, :]), score_view(t), axis=AX.X, op=ALU.max))
        dve(("mx", t), [("rowmax", t), "late"] + ([("sumexp", t - 2)] if t >= 2 else []), lambda e: e.tensor_tensor(
            st[:, 0, :], st[:, 0, :], sink[:, :, :].rearrange("p g a -> p (g a)"), ALU.max))
        dve(("shift", t), [("mx", t)] + ([("pt", t - 2)] if t >= 2 else []), lambda e: e.tensor_tensor(
            pr[:, :, :].rearrange("p (g a) k -> p g a k", g=4), score_view(t),
            four(st[:, 0, :]).unsqueeze(3).to_broadcast([P, 4, 4, T]), ALU.subtract))
        dve(("sinkd", t), [("mx", t)], lambda e: e.tensor_tensor(
            st[:, 1, :], sink[:, :, :].rearrange("p g a -> p (g a)"), st[:, 0, :], ALU.subtract))
        act(("exp", t), [("shift", t)], lambda e: e.activation(pr[:, :, :], pr[:, :, :], ACT.Exp))
        act(("sinkexp", t), [("sinkd", t)], lambda e: e.activation(st[:, 2, :], st[:, 1, :], ACT.Exp))

    def softmax_b(t):
        st, pr = stat[t % 2], prob[t % 2]
        dve(("sums", t), [("exp", t)], lambda e: e.tensor_reduce(st[:, 3, :], pr[:, :, :], axis=AX.X, op=ALU.add))
        dve(("sumexp", t), [("sums", t), ("sinkexp", t)], lambda e: e.tensor_tensor(
            st[:, 3, :], st[:, 3, :], st[:, 2, :], ALU.add))
        dve(("rden", t), [("sumexp", t)], lambda e: e.reciprocal(st[:, 4, :], st[:, 3, :]))
        dve(("norm", t), [("rden", t)], lambda e: e.tensor_tensor(
            pr[:, :, :], pr[:, :, :], st[:, 4, :].unsqueeze(2).to_broadcast([P, 16, T]), ALU.mult))

    def turn_prob(t):
        pr = prob[t % 2]
        for hb in range(2):
            u, bank, free = banks.take()
            for n in range(4):
                at = hb * 4 + n
                pe(("pt", t) if at == 7 else ("pt0", t) if at == 3 else None, [("norm", t), "late"] + free,
                   lambda e, b=bank, n=n, at=at: e.transpose(
                       b[:, n * P:(n + 1) * P], pr[:, 2 * at:2 * at + 2, :].rearrange("p a k -> p (a k)"), ident[:, :]))
            act(("pt_s", t, hb), [("pt", t) if hb else ("pt0", t)] + ([("pv", t - 1)] if t else []),
                lambda e, b=bank, hb=hb: e.activation(
                    prob_t[:, 2 * hb:2 * hb + 2, :], b[:, :].rearrange("p (g n) -> p g n", g=2), ACT.Copy))
            banks.read_by(u, ("pt_s", t, hb))

    def attend(t):
        m, s = divmod(t, TPM)
        took = [banks.take() for _ in range(2)]
        for gp in range(2):
            for go in range(2):
                for b in range(2):
                    g, (u, bank, free) = 2 * gp + go, took[b]
                    rows = slice(b * T, (b + 1) * T)
                    pe(("pv", t) if gp == go == b == 1 else None,
                       [("pt_s", t, 0), ("pt_s", t, 1), ("v_s", m, s)] + free,
                       lambda e, bank=bank, g=g, gp=gp, go=go, rows=rows, b=b: e.matmul(
                           bank[go * DH:(go + 1) * DH, gp * 256:(gp + 1) * 256],
                           v_s[m % 2][rows, s, g * DH:(g + 1) * DH], prob_t[rows, g, :],
                           start=True, stop=True, tile_position=(b * T, go * DH)))
        for b in range(2):
            act(("y_t", t, b), [("pv", t)] + ([("proj", t - 1)] if t else []), lambda e, b=b: e.activation(
                y_t[:, :, :, b, :].rearrange("p g j s -> p (g j) s"),
                took[b][1][:, :].rearrange("p (c s) -> p c s", s=T), ACT.Copy))
            banks.read_by(took[b][0], ("y_t", t, b))

    def project(t):
        m, s = divmod(t, TPM)
        i = m % 2
        u, bank, free = banks.take()
        for n in range(2 * REP):
            pe(None, [("y_t", t, 0), ("y_t", t, 1), "late"] + free, lambda e, b=bank, n=n: e.matmul(
                b[:, 0:D], y_t[:, n // REP, n % REP, :, :].rearrange("p b s -> p (b s)"), w_o[:, n, :],
                start=n == 0, stop=False))
        for c in range(KC):
            pe(("proj", t) if c == KC - 1 else None, [("x0", m, c)], lambda e, b=bank, c=c: e.matmul(
                b[:, c * P:(c + 1) * P], x0_t[i][:, c, s * P:(s + 1) * P], ident[:, :],
                start=False, stop=c == KC - 1))
        dve(("x2", t), [("proj", t)] + ([("h2", t - 2 * TPM), ("resid", t - 2 * TPM)] if m >= 2 else []),
            lambda e, b=bank: e.tensor_tensor(x2[i][:, s, :], b[:, 0:D], b_o[:, :], ALU.add))
        banks.read_by(u, ("x2", t))
        pool(("resid", t), [("x2", t), "resid_x"], lambda e: e.tensor_tensor(
            resid[:, t, :], resid[:, t, :], x2[i][:, s, :], ALU.add))
        act(("ssq2", t), [("x2", t)] + ([("rms2", m - 2)] if m >= 2 else []) + ([("ssq2", t - 1)] if t else []),
            lambda e: e.activation(
            sq_scrap[:, :], x2[i][:, s, :], ACT.Square, accum_out=ssq[i][:, s:s + 1]))

    def root2(m):
        act(("root2", m), [("ssq2", TPM * m + TPM - 1), "ones"], lambda e: e.activation(
            ssq[m % 2][:, :], ssq[m % 2][:, :], ACT.Sqrt, bias=eps[:, 0:1], scale=1.0 / D))
        dve(("rms2", m), [("root2", m)] + ([("h2", TPM * (m - 1) - 1)] if m >= 2 else []), lambda e: e.reciprocal(
            rms2[m % 2][:, :], ssq[m % 2][:, :]))

    def route_a(t):
        m, s = divmod(t, TPM)
        i, hb, pb = m % 2, t % 2, t % NPAY
        free = [("h2_stored", t - 2), ("h2_turn", t - 2)] if t >= 2 else []
        dve(("h2", t), [("rms2", m), ("x2", t), "late"] + free, lambda e: e.scalar_tensor_tensor(
            out=h2[hb][:, :], in0=x2[i][:, s, :], scalar=rms2[i][:, s:s + 1], in1=norm2_w[:, :],
            op0=ALU.mult, op1=ALU.mult))
        dma("sync", ("h2_stored", t), [("h2", t)], s_h2[hb], 16 * (t // 2 + 1),
            h2_rows[t * P:(t + 1) * P, :], h2[hb][:, :])
        u, bank, free = banks.take()
        for c in range(KC):
            pe(("h2_turn", t) if c == KC - 1 else None, [("h2", t), "late"] + free, lambda e, b=bank, c=c: e.transpose(
                b[:, c * P:(c + 1) * P], h2[hb][:, c * P:(c + 1) * P], ident[:, :]))
        act(("h2_t", t), [("h2_turn", t)] + ([("gate", t - 1)] if t else []), lambda e, b=bank: e.activation(
            h2_t[:, :, :], b[:, 0:D].rearrange("p (c n) -> p c n", c=KC), ACT.Copy))
        banks.read_by(u, ("h2_t", t))

    def route_b(t):
        pb = t % NPAY
        u, bank, free = banks.take()
        for c in range(KC):
            pe(("gate", t) if c == KC - 1 else None, [("h2_t", t)] + free, lambda e, b=bank, c=c: e.matmul(
                b[:, 0:E], h2_t[:, c, :], w_gate[:, c, :], start=c == 0, stop=c == KC - 1))
        dve(("glog", t), [("gate", t), "late"], lambda e, b=bank: e.tensor_tensor(
            glog[:, :], b[:, 0:E], b_gate[:, :], ALU.add))
        dve(("top", t), [("glog", t)], lambda e: e.max(top[:, :], glog[:, :]))
        dve(("top_i", t), [("top", t)], lambda e: e.max_index(top_i[:, :], top[:, :], glog[:, :]))
        dve(("gsub", t), [("top", t)] + ([("gexp", t - 1)] if t else []), lambda e: e.tensor_scalar(
            gexp[:, :], top[:, 0:TOPK], top[:, 0:1], None, ALU.subtract))
        act(("gexp", t), [("gsub", t)], lambda e: e.activation(
            gexp[:, :], gexp[:, :], ACT.Exp, accum_out=gsum[:, 0:1]))
        dve(("top_f", t), [("top_i", t)], lambda e: e.tensor_copy(top_f[:, :], top_i[:, 0:TOPK]))
        dve(("onehot", t), [("top_f", t), "late"], lambda e: e.tensor_tensor(
            onehot[:, :, :], expert_no[:, :].unsqueeze(1).to_broadcast([P, TOPK, E]),
            top_f[:, :].unsqueeze(2).to_broadcast([P, TOPK, E]), ALU.is_equal))

        def all_picks(e):
            with nc.allow_low_precision("sums of 0 and 1"):
                return e.tensor_reduce(picked[:, :], onehot[:, :, :].rearrange("p k n -> p n k"), axis=AX.X, op=ALU.add)
        dve(("picked", t), [("onehot", t)] + ([("count", t - 1)] if t else []), all_picks)
        pe(None, [("picked", t), "consts_b"], lambda e, b=bank: e.matmul(
            b[:, 64:64 + E], earlier[:, :], picked[:, :], start=True, stop=True))
        pe(("count", t), ["ones"], lambda e, b=bank: e.matmul(
            b[:, 128:128 + E], ones_b[:, :], picked[:, :], start=True, stop=True))
        dve(("grecip", t), [("gexp", t)], lambda e: e.reciprocal(gsum[:, 1:2], gsum[:, 0:1]))
        free = [("listed", t - NPAY)] if t >= NPAY else []
        dve(("gates", t), [("grecip", t)] + free, lambda e: e.tensor_scalar(
            entry[pb][:, :, 1], gexp[:, :], gsum[:, 1:2], None, ALU.mult))
        dve(("ids", t), [], lambda e: e.tensor_scalar(
            entry[pb][:, :, 0], pair_no[:, :], float(TOPK * P * t), None, ALU.add))
        dve(("rank", t), [("count", t)] + ([("filled", t - 1)] if t else []), lambda e, b=bank: e.tensor_tensor(
            rank[:, :], b[:, 64:64 + E], filled[:, :], ALU.add))
        dve(("slots", t), [("rank", t)], lambda e: e.tensor_tensor(
            onehot_s[:, :, :], onehot[:, :, :], rank[:, :].unsqueeze(1).to_broadcast([P, TOPK, E]), ALU.mult))
        dve(("filled", t), [("rank", t)], lambda e, b=bank: e.tensor_tensor(
            filled[:, :], filled[:, :], b[:, 128:128 + E], ALU.add))
        banks.read_by(u, ("filled", t))
        dve(("slot_f", t), [("slots", t)], lambda e: e.tensor_reduce(
            slot_f[:, :], onehot_s[:, :, :], axis=AX.X, op=ALU.add))
        dve(("slot_i", t), [("slot_f", t)], lambda e: e.tensor_copy(slot_i[pb][:, :], slot_f[:, :]))
        for k in range(TOPK):
            plan.put("gpsimd", ("listed", t), [("slot_i", t), ("ids", t), "fill"],
                     lambda e, k=k: e.indirect_dma_start(
                         out=lists, out_offset=bass.IndirectOffsetOnAxis(ap=slot_i[pb][:, k:k + 1], axis=0),
                         in_=entry[pb][:, k, :], in_offset=None),
                     s_entry[pb], 16, 16 * TOPK * (t // NPAY + 1))

    down(0)
    up(0)
    norm1(0)
    for j in range(NPAIR):
        pair(0, j)
    for s in range(TPM):
        value(0, s)
    score(0)
    softmax_a(0)
    softmax_b(0)
    for m in range(NM):
        n = m + 1
        nxt = n < NM
        units = [[lambda: down(n), lambda: up(n), lambda: norm1(n)],
                 [lambda: pair(n, 0), lambda: pair(n, 1), lambda: pair(n, 2)],
                 [lambda: pair(n, 3), lambda: pair(n, 4), lambda: value(n, 0)],
                 [lambda: value(n, 1), lambda: value(n, 2), lambda: value(n, 3)]]
        for s in range(TPM):
            t = m * TPM + s
            if t + 1 < NT:
                score(t + 1)
                softmax_a(t + 1)
            if nxt:
                units[s][0]()
            turn_prob(t)
            if t + 1 < NT:
                softmax_b(t + 1)
            if nxt:
                units[s][1]()
            attend(t)
            if nxt:
                units[s][2]()
            elif s == 0:
                root2(m - 1)
            if m:
                route_a(t - TPM)
            project(t)
            if m:
                route_b(t - TPM)
        if n + 1 < NM:
            load_x_t(n + 1)
    root2(NM - 1)
    for s in range(TPM):
        route_a((NM - 1) * TPM + s)
        route_b((NM - 1) * TPM + s)

    part1.close()
    tiles_f = [sb(f"tiles_f{i}", [P, E]) for i in range(2)]
    tiles_i = sb("tiles_i", [P, E], I32)
    tiles_n = sb("tiles_n", [P, E])
    ended = sb("ended", [P, 2, E])
    ended_n = sb("ended_n", [P, 2, E])
    of_tile = sb("of_tile", [P, 4, 2])
    list_tile = sb("list_tile", [P, 2], I32)
    rows_of = sb("rows_of", [P, 2, 2 * P])
    ids_f = sb("ids_f", [P, P + NET2])
    gates = sb("gates", [P, P + NET2])
    pair_row = sb("pair_row", [P, P + NET2], I32)
    token_row = sb("token_row", [P, P + NET2], I32)
    plan_f = sb("plan_f", [1, 2 * P])
    plan_e = sb("plan_e", [1, 2 * P], I32)
    plan_slot = sb("plan_slot", [1, 2 * P], I32)
    plan_wait = sb("plan_wait", [1, 2 * P], I32)
    ring_wait = sb("ring_wait", [1, E], I32)
    NG = 6
    rows_in = [sb(f"rows_in{i}", [P, D]) for i in range(NG)]
    in_t = [sb(f"in_t{i}", [P, KC, P]) for i in range(2)]
    silu = [sb(f"silu{i}", [P, DFF]) for i in range(2)]
    mid = [sb(f"mid{i}", [P, DFF]) for i in range(2)]
    mid_t = [sb(f"mid_t{i}", [P, FC, P]) for i in range(2)]
    NY = 4
    rows_out = [sb(f"rows_out{i}", [P, D]) for i in range(NY)]
    NC = 4
    picks = [sb(f"picks{i}", [P, TOPK, D]) for i in range(NC)]
    s_rows = [sem(f"s_rows{i}") for i in range(2)]
    s_in = [sem(f"s_in{i}") for i in range(NG)]
    s_put = [sem(f"s_put{i}") for i in range(NY)]
    s_w = [sem(f"s_w{i}") for i in range(RING)]
    s_wready = sem("s_wready")
    s_used = sem("s_used")
    s_picks = [sem(f"s_picks{i}") for i in range(NC)]
    s_out = sem("s_out")

    last = NT - 1
    p1_done = [("count", last), ("slot_i", last), ("gexp", last)] + [("listed", last - i) for i in range(NPAY)]
    every_h2 = [("h2_stored", last), ("h2_stored", last - 1)]

    dve("z0", p1_done + [("filled", last)], lambda e: e.tensor_tensor(
        tiles_f[0][:, :], filled[:, :], list_base[:, :], ALU.subtract))
    dve("z1", ["z0"], lambda e: e.tensor_scalar(tiles_i[:, :], tiles_f[0][:, :], float(P - 1), None, ALU.add))
    dve("z1s", ["z1"], lambda e: e.tensor_scalar(tiles_i[:, :], tiles_i[:, :], 7, None, ALU.arith_shift_right))
    dve("z2", ["z1s"], lambda e: e.tensor_scalar(tiles_i[:, :], tiles_i[:, :], 1, None, ALU.max))
    dve("z3", ["z2"], lambda e: e.tensor_copy(tiles_n[:, :], tiles_i[:, :]))
    dve("sum0", ["z2"], lambda e: e.tensor_copy(tiles_f[0][:, :], tiles_i[:, :]))
    steps = 0
    while 1 << steps < E:
        w = 1 << steps
        a, b = tiles_f[steps % 2], tiles_f[1 - steps % 2]
        dve(None, [f"sum{steps}"], lambda e, a=a, b=b, w=w: e.tensor_copy(b[:, 0:w], a[:, 0:w]))
        steps += 1
        dve(f"sum{steps}", [], lambda e, a=a, b=b, w=w: e.tensor_tensor(b[:, w:E], a[:, w:E], a[:, 0:E - w], ALU.add))
    ends = tiles_f[steps % 2]
    dve("ring_wait", [f"sum{steps}"], lambda e: e.tensor_scalar(ring_wait[:, :], ends[0:1, :], 1.0, None, ALU.add))
    dve("y0", [f"sum{steps}"], lambda e: e.tensor_tensor(
        ended[:, :, :], ends[:, :].unsqueeze(1).to_broadcast([P, 2, E]),
        tile_no[:, :].unsqueeze(2).to_broadcast([P, 2, E]), ALU.is_le))
    dve("y1", ["y0", "z3"], lambda e: e.tensor_tensor(
        ended_n[:, :, :], ended[:, :, :], tiles_n[:, :].unsqueeze(1).to_broadcast([P, 2, E]), ALU.mult))
    dve("y2", ["y0"], lambda e: e.tensor_reduce(of_tile[:, 0, :], ended[:, :, :], axis=AX.X, op=ALU.add))
    dve("y3", ["y1"], lambda e: e.tensor_reduce(of_tile[:, 1, :], ended_n[:, :, :], axis=AX.X, op=ALU.add))
    dve("y4", ["y3"], lambda e: e.tensor_tensor(of_tile[:, 1, :], tile_no[:, :], of_tile[:, 1, :], ALU.subtract))
    dve("y5", ["y4", "y2"], lambda e: e.scalar_tensor_tensor(
        out=of_tile[:, 2, :], in0=of_tile[:, 0, :], scalar=float(LT), in1=of_tile[:, 1, :],
        op0=ALU.mult, op1=ALU.add))
    dve("list_tile", ["y5"], lambda e: e.tensor_scalar(
        list_tile[:, :], of_tile[:, 2, :], float(E * LT), None, ALU.min))
    dve("expert", ["y2"], lambda e: e.tensor_scalar(of_tile[:, 3, :], of_tile[:, 0, :], float(E - 1), None, ALU.min))
    for h in range(2):
        pe("plan_row" if h else None, ["expert", ("filled", last)], lambda e, h=h: e.matmul(
            gbank[0][0:1, h * P:(h + 1) * P], of_tile[:, 3, h:h + 1], ident[:, :], start=True, stop=True))
    dve("plan_e", ["plan_row"], lambda e: e.tensor_copy(plan_e[:, :], gbank[0][0:1, 0:2 * P]))
    dve("plan_slot", ["plan_e"], lambda e: e.tensor_scalar(
        plan_slot[:, :], plan_e[:, :], RING - 1, None, ALU.bitwise_and))
    dve("plan_wait", ["plan_row"], lambda e: e.tensor_scalar(
        plan_wait[:, :], gbank[0][0:1, 0:2 * P], 1.0, None, ALU.add))
    list_rows = lists.rearrange("(t r) w -> t (r w)", r=P)
    for h, n in ((0, P), (1, NET2)):
        plan.put("gpsimd", ("entries", h), ["list_tile", *p1_done], lambda e, h=h, n=n: e.indirect_dma_start(
            out=rows_of[0:n, h, :], out_offset=None, in_=list_rows,
            in_offset=bass.IndirectOffsetOnAxis(ap=list_tile[0:n, h:h + 1], axis=0)), s_rows[h], 16, 16)
        for w in range(2):
            pe(("turned", h, w), [("entries", h), ("x2", last), ("h2_t", last)], lambda e, h=h, n=n, w=w: e.transpose(
                gbank[1 + w][:, h * P:h * P + n],
                rows_of[0:n, h, :].rearrange("p (r w) -> p w r", w=2)[:, w, :], ident[0:n, 0:n]))
    dve("pair_row", [("turned", 1, 0)], lambda e: e.tensor_copy(pair_row[:, :], gbank[1][:, 0:P + NET2]))
    dve("gates2", [("turned", 1, 1)], lambda e: e.tensor_copy(gates[:, :], gbank[2][:, 0:P + NET2]))
    dve("tok0", ["pair_row"], lambda e: e.tensor_scalar(
        token_row[:, :], pair_row[:, :], 2, None, ALU.arith_shift_right))
    dve("token_row", ["tok0"], lambda e: e.tensor_scalar(token_row[:, :], token_row[:, :], NTOK - 1, None, ALU.min))

    pe(None, [], lambda e: e.sem_inc(s_used, 1))

    def load_expert(e_no, after):
        r = e_no % RING
        at = ring[:, r * WE:(r + 1) * WE]
        name = ("w", e_no)
        up_, down_ = at[:, 0:KC * 2 * DFF], at[:, KC * 2 * DFF:WE]
        plan.put("sync", name, after, lambda e: e.dma_start(
            up_.rearrange("p (c n) -> p c n", c=KC), d["W_up"][e_no].rearrange("(c p) n -> p c n", p=P)),
            s_w[r], 16, 32 * (e_no // RING + 1))
        plan.put("sync", name, [], lambda e: e.dma_start(
            down_.rearrange("p (c n) -> p c n", c=FC), d["W_down"][e_no].rearrange("(c p) n -> p c n", p=P)),
            s_w[r], 16, 32 * (e_no // RING + 1))

    def say_ready(e_no):
        plan.put("sync", ("ready", e_no), [("w", e_no)], lambda e: e.nop(), s_wready, 1, e_no + 1)

    for e_no in range(RING):
        load_expert(e_no, [])
    for e_no in range(RING - 1):
        say_ready(e_no)
    for e_no in range(RING, E):
        def wait_used(e, k=e_no - RING):
            v = e.value_load(ring_wait[0:1, k:k + 1], min_val=1, max_val=NET + 1)
            e.wait_ge(s_used, v)
            return e.nop()
        plan.put("sync", None, ["ring_wait"], wait_used)
        load_expert(e_no, [])
        say_ready(e_no - 1)
    say_ready(E - 1)

    def gather(i):
        free = [("in_turn", i - NG)] if i >= NG else p1_done
        plan.put("gpsimd", ("rows", i), ["token_row", *every_h2, *free], lambda e: e.indirect_dma_start(
            out=rows_in[i % NG][:, :], out_offset=None, in_=h2_rows,
            in_offset=bass.IndirectOffsetOnAxis(ap=token_row[:, i:i + 1], axis=0)),
            s_in[i % NG], 16, 16 * (i // NG + 1))

    def scatter(i):
        plan.put("gpsimd", ("put", i), [("y", i), "pair_row"], lambda e: e.indirect_dma_start(
            out=pick_rows, out_offset=bass.IndirectOffsetOnAxis(ap=pair_row[:, i:i + 1], axis=0),
            in_=rows_out[i % NY][:, :], in_offset=None, bounds_check=PAIRS - 1, oob_is_err=False),
            s_put[i % NY], 16, 16 * (i // NY + 1))

    free_of_part1 = ["gates2", "plan_wait", "pair_row", ("shift", last), ("v_s", NM - 1, TPM - 1)]

    def turn_in(i):
        bank = scores[:, i % 2, 0:D]
        for c in range(KC):
            pe(("in_turn", i) if c == KC - 1 else None,
               [("rows", i)] + ([("in_t", i - 2)] if i >= 2 else free_of_part1),
               lambda e, c=c: e.transpose(bank[:, c * P:(c + 1) * P],
                                          rows_in[i % NG][:, c * P:(c + 1) * P], ident[:, :]))
        dve(("in_t", i), [("in_turn", i)] + ([("ug", i - 2)] if i >= 2 else []), lambda e: e.tensor_copy(
            in_t[i % 2][:, :, :], bank.rearrange("p (c n) -> p c n", c=KC)))

    slot_of = {}

    def expert_up(i):
        bank = gbank[i % 2]

        def first(e):
            if i % 4 == 0:
                for k in range(i, min(i + 4, NET)):
                    slot_of[k] = (e.value_load(plan_slot[0:1, k:k + 1], min_val=0, max_val=RING - 1),
                                  e.value_load(plan_wait[0:1, k:k + 1], min_val=1, max_val=E))
            e.wait_ge(s_wready, slot_of[i][1])
            return mm(e, 0)

        def mm(e, c):
            return e.matmul(bank[:, :], in_t[i % 2][:, c, :],
                            ring[:, bass.ds(slot_of[i][0] * WE + c * 2 * DFF, 2 * DFF)], start=c == 0, stop=c == KC - 1)
        pe(None, [("in_t", i), "plan_slot", "plan_wait"] + ([("mid", i - 2), ("silu", i - 2)] if i >= 2 else free_of_part1), first)
        pe(("ug", i), [], lambda e: mm(e, 1))
        act(("silu", i), [("ug", i)] + ([("mid", i - 2)] if i >= 2 else []), lambda e: e.activation(
            silu[i % 2][:, :], bank[:, DFF:2 * DFF], ACT.Silu))
        dve(("mid", i), [("silu", i)] + ([("mid_turn", i - 2)] if i >= 2 else []), lambda e: e.tensor_tensor(
            mid[i % 2][:, :], silu[i % 2][:, :], bank[:, 0:DFF], ALU.mult))

    def turn_mid(i):
        bank = scores[:, 2 + i % 2, 0:D]
        for c in range(FC):
            pe(("mid_turn", i) if c == FC - 1 else None, [("mid", i)] + ([("mid_t", i - 2)] if i >= 2 else []),
               lambda e, c=c: e.transpose(bank[:, c * P:(c + 1) * P],
                                          mid[i % 2][:, c * P:(c + 1) * P], ident[:, :]))
        dve(("mid_t", i), [("mid_turn", i)] + ([("yd", i - 2)] if i >= 2 else []), lambda e: e.tensor_copy(
            mid_t[i % 2][:, :, :], bank.rearrange("p (c n) -> p c n", c=FC)))

    def expert_down(i):
        out = gbank[2 + i % 2][:, 0:D]
        for c in range(FC):
            def mm(e, c=c):
                ins = e.matmul(out, mid_t[i % 2][:, c, :],
                               ring[:, bass.ds(slot_of[i][0] * WE + KC * 2 * DFF + c * D, D)],
                               start=c == 0, stop=c == FC - 1)
                return ins
            after = [("mid_t", i)] + ([("y", i - 2)] if i >= 2 else [])
            if c < FC - 1:
                pe(None, after, mm)
            else:
                plan.put("tensor", ("yd", i), after, mm, s_used, 1, i + 2)
        act(("y", i), [("yd", i)] + ([("put", i - NY)] if i >= NY else []), lambda e: e.activation(
            rows_out[i % NY][:, :], out, ACT.Copy, scale=gates[:, i:i + 1]))

    for i in range(NG - 1):
        gather(i)
    turn_in(0)
    for i in range(NET + 1):
        if i + NG - 1 < NET:
            gather(i + NG - 1)
        if i + 1 < NET:
            turn_in(i + 1)
        if i < NET:
            expert_up(i)
        if i >= 1:
            turn_mid(i - 1)
            expert_down(i - 1)
            scatter(i - 1)

    every_put = [("put", NET - 1 - k) for k in range(NY)]
    for t in range(NT):
        pk = picks[t % NC]
        dma("sync", ("picks", t), (every_put if t < NC else [("final", t - NC)]), s_picks[t % NC], 16 * (t // NC + 1),
            pk[:, :, :], pick_rows[t * P * TOPK:(t + 1) * P * TOPK, :].rearrange("(p k) n -> p k n", k=TOPK))
        dve(("half", t), [("picks", t)], lambda e, pk=pk: e.tensor_tensor(
            pk[:, 0:2, :], pk[:, 0:2, :], pk[:, 2:4, :], ALU.add))
        dve(("whole", t), [("half", t)], lambda e, pk=pk: e.tensor_tensor(
            pk[:, 0, :], pk[:, 0, :], pk[:, 1, :], ALU.add))
        dve(("final", t), [("whole", t), ("resid", t)], lambda e, pk=pk, t=t: e.tensor_tensor(
            resid[:, t, :], resid[:, t, :], pk[:, 0, :], ALU.add))
        dma("scalar", "out", [("final", t)], s_out, 16 * NT, d["out"][t * P:(t + 1) * P, :], resid[:, t, :])
    plan.put("scalar", None, ["out"], lambda e: e.nop())

    plan.settle(engine_sem)
    with ctx:
        block = ctx.enter_context(nc.Block())

        @block.sync
        def _(e):
            plan.emit("sync", e)

        @block.scalar
        def _(e):
            plan.emit("scalar", e)

        @block.vector
        def _(e):
            plan.emit("vector", e)

        @block.gpsimd
        def _(e):
            plan.emit("gpsimd", e)

        @block.tensor
        def _(e):
            plan.emit("tensor", e)


def _constants():
    f = np.float32
    p = np.arange(P)
    pos = np.arange(T, dtype=f) / f(32.0)
    inv = (f(1.0) / np.power(f(150000.0), np.arange(0, DH, 2, dtype=f) / f(DH))).astype(f)
    angle = (pos[:, None] * inv[None, :]).astype(f)
    cos, sin = np.cos(angle).T[p % 32], np.sin(angle).T[p % 32]
    scale = f(DH ** -0.5)
    return {
        "rope": np.stack([cos * scale, sin * scale, cos, sin], 1).astype(f),
        "causal": np.where(np.arange(T)[None, :] > (p % T)[:, None], f(NEG), f(0)).astype(f),
        "ident": np.eye(P, dtype=f),
        "earlier": (p[:, None] < p[None, :]).astype(f),
        "expert_no": np.tile(np.arange(E, dtype=f), (P, 1)),
        "list_base": np.tile(np.arange(E, dtype=f) * LIST, (P, 1)),
        "pair_no": (TOPK * p[:, None] + np.arange(TOPK)[None, :]).astype(f),
        "tile_no": np.stack([p, p + P], 1).astype(f),
        "fill_slots": np.tile(np.stack([PAIRS + p, 0 * p], 1).astype(f)[None], (P, 1, 1)),
    }


def kernel(**inputs):
    import concourse.bacc as bacc
    from concourse.bass_utils import run_bass_kernel_spmd

    a = {n: np.asarray(v) for n, v in inputs.items()}
    wide = lambda v: np.ascontiguousarray(np.broadcast_to(v, (P, v.shape[-1])))
    cols = []
    for j in range(NPAIR):
        for o in range(2):
            for g in range(KV):
                head = (REP * g + j) * DH if j < REP else H * DH + g * DH
                cols += list(head + 2 * np.arange(DH // 2) + o)
    cols = np.array(cols)
    qkv_w, qkv_b = a["L0_ffn_qkv_w"], a["L0_ffn_qkv_b"]
    rows = np.concatenate([(REP * (2 * gp + go) + j) * DH + np.arange(DH)
                           for gp in range(2) for j in range(REP) for go in range(2)])
    heads = np.array([[REP * g + 2 * pa + q // T for g in range(KV) for pa in range(2) for _ in range(2)]
                      for q in range(P)])
    arrays = {
        "x": a["x"].reshape(NTOK, D),
        "x_t": a["x"].reshape(NTOK, D).T,
        "cond_t": a["cond_512"].T,
        "g_down": a["L0_cond_down_gamma"], "b_down": a["L0_cond_down_beta"],
        "g_up": a["L0_cond_up_gamma"], "b_up": a["L0_cond_up_beta"],
        "w_down": a["L0_cond_down_project"], "w_up": a["L0_cond_up_project"],
        "norm1_w": a["L0_ffn_attn_norm_w"].reshape(KC, P).T,
        "norm2_w": wide(a["L0_ffn_ffn_norm_w"]),
        "w_qk": qkv_w[:, cols], "b_qk": qkv_b[cols].reshape(NPAIR * 2, P).T,
        "w_v": qkv_w[:, (H + KV) * DH:], "b_v": wide(qkv_b[(H + KV) * DH:]),
        "w_o": a["L0_ffn_proj_w"][rows], "b_o": wide(a["L0_ffn_proj_b"]),
        "sink": a["L0_ffn_attn_sink"][heads].reshape(P, 4, 4),
        "w_gate": a["L0_ffn_gate_w"], "b_gate": wide(a["L0_ffn_gate_b"]),
        "W_up": a["L0_ffn_W_up"], "W_down": a["L0_ffn_W_down"],
        **_constants(),
    }
    nc = bacc.Bacc("TRN2", target_bir_lowering=False, num_devices=1)
    sent, d = {}, {}
    for name, v in arrays.items():
        v = np.ascontiguousarray(v)
        sent["in_" + name] = v
        d[name] = nc.dram_tensor("in_" + name, v.shape, mybir.dt.from_np(v.dtype), kind="ExternalInput").ap()
    d["out"] = nc.dram_tensor("out_0", (NTOK, D), F32, kind="ExternalOutput").ap()
    program(nc, d)
    r = run_bass_kernel_spmd(nc, [sent], core_ids=[0])
    return r.results[0]["out_0"].reshape(NSEQ, T, D)
```
